# Optimizing a Trainium2 kernel written in Bass

```python
import numpy as np
import jax
import jax.numpy as jnp

def _softmax(x, axis=-1):
    return jax.nn.softmax(x, axis=axis)

def _gelu(x):
    return jax.nn.gelu(x, approximate=True)

def _silu(x):
    return jax.nn.silu(x)

def _sigmoid(x):
    return jax.nn.sigmoid(x)

def _layernorm(x, axis=-1, eps=1e-05):
    m = jnp.mean(x, axis=axis, keepdims=True)
    v = jnp.var(x, axis=axis, keepdims=True)
    return (x - m) / jnp.sqrt(v + eps)

def _scatter_add(tgt, idx, src, axis=0):
    return tgt.at[idx].add(src)

def _segment_sum(src, seg, n):
    return jax.ops.segment_sum(src, seg, n)
kernel_name = 'mk_cond_resid_d2_seqx_r4_fd4b69'

def setup_inputs(seed: int=0):
    np.random.seed(seed)
    _w = jnp.asarray

    def _rec_inputs():
        import jax
        import jax.numpy as jnp
        _rk = jax.random.key(seed)
        x = -0.000125 + 0.9999 * jax.random.normal(jax.random.fold_in(_rk, 1), (4, 512, 256), jnp.float32)
        _lenS = 512 - jax.random.randint(jax.random.fold_in(_rk, 7), (4,), 0, max(1, 512 // 4) + 1, jnp.int32)
        _lenS2 = 512 - jax.random.randint(jax.random.fold_in(_rk, 8), (4,), 0, max(1, 512 // 4) + 1, jnp.int32)
        cond_1024 = 0.00513981 + 1.0024 * jax.random.normal(jax.random.fold_in(_rk, 11), (4, 256), jnp.float32)
        return (x, cond_1024)
    x, cond_1024 = _rec_inputs()

    def _L0_cond_setup():
        import jax, jax.numpy as jnp
        import numpy as np
        IN_FEATURES = 256
        OUT_FEATURES = 256
        BATCH = 32
        SEQ = 256
        EPS = 1e-08
        key = jax.random.key(seed)
        k1, k2, k3 = jax.random.split(key, 3)
        Efou = jax.random.normal(k1, (BATCH, SEQ, IN_FEATURES), dtype=jnp.float32)
        y = jax.random.normal(k2, (BATCH, IN_FEATURES), dtype=jnp.float32)
        weight = jax.random.normal(k3, (IN_FEATURES, OUT_FEATURES), dtype=jnp.float32)
        return {'Efou': Efou, 'y': y, 'weight': weight}
    _L0_cond_all = _L0_cond_setup()
    _L0_cond_in = {k: v for k, v in _L0_cond_all.items() if k in ('weight',)}
    del _L0_cond_all

    def _L1_cond_setup():
        import jax, jax.numpy as jnp
        import numpy as np
        N, T, D, H = (128, 128, 256, 256)
        key = jax.random.key(seed)
        k1, k2, k3, k4 = jax.random.split(key, 4)
        x = jax.random.normal(k1, (N, T, D), dtype=jnp.float32)
        h0 = jax.random.normal(k2, (N, H), dtype=jnp.float32)
        Wx = jax.random.normal(k3, (D, H), dtype=jnp.float32) / np.sqrt(D)
        Wh = jax.random.normal(k4, (H, H), dtype=jnp.float32) / np.sqrt(H)
        b = jnp.zeros((H,), dtype=jnp.float32)
        return {'x': x, 'h0': h0, 'Wx': Wx, 'Wh': Wh, 'b': b}
    _L1_cond_all = _L1_cond_setup()
    _L1_cond_in = {k: v for k, v in _L1_cond_all.items() if k in ('Wx', 'Wh', 'b')}
    del _L1_cond_all
    return {'x': x, 'cond_1024': cond_1024, 'L0_cond_weight': _L0_cond_in['weight'], 'L1_cond_Wx': _L1_cond_in['Wx'], 'L1_cond_Wh': _L1_cond_in['Wh'], 'L1_cond_b': _L1_cond_in['b']}

def reference(x, cond_1024, L0_cond_weight, L1_cond_Wx, L1_cond_Wh, L1_cond_b):
    import jax
    import jax.numpy as jnp

    def _L0_cond_ref(Efou, y, weight):
        import jax, jax.numpy as jnp
        import numpy as np
        IN_FEATURES = 256
        OUT_FEATURES = 256
        BATCH = 32
        SEQ = 256
        EPS = 1e-08
        scale = 1.0 / np.sqrt(np.float32(weight.shape[0]))
        ys = y * scale
        d = jax.lax.rsqrt(jnp.einsum('bi,io->bo', ys * ys, weight * weight) + EPS)
        out = jnp.einsum('bsi,io->bso', Efou * ys[:, None, :], weight) * d[:, None, :]
        return out

    def _L1_cond_ref(x, h0, Wx, Wh, b):
        import jax, jax.numpy as jnp
        import numpy as np
        N, T, D, H = (128, 128, 256, 256)
        xp = jnp.einsum('ntd,dh->nth', x, Wx) + b

        def step(prev_h, xp_t):
            next_h = jnp.tanh(xp_t + prev_h @ Wh)
            return (next_h, next_h)
        _, hs = jax.lax.scan(step, h0, jnp.swapaxes(xp, 0, 1))
        return jnp.swapaxes(hs, 0, 1)
    x = x + _L0_cond_ref(x, cond_1024, L0_cond_weight)
    x = x + _L1_cond_ref(x, cond_1024, L1_cond_Wx, L1_cond_Wh, L1_cond_b)
    return x

_drawn_inputs = setup_inputs


def setup_inputs(seed=0):
    import zlib

    import numpy as np

    out = dict(_drawn_inputs(seed))
    spreads = {'L1_cond_b': (0.0, 0.1)}
    factors = {}
    for name, (base, spread) in spreads.items():
        noise = np.random.default_rng([zlib.crc32(name.encode()), seed]).standard_normal(out[name].shape)
        drawn = base * np.exp(spread * noise) if base else spread * noise
        out[name] = jnp.asarray(drawn.astype(out[name].dtype))
    for name, factor in factors.items():
        out[name] = (out[name] * factor).astype(out[name].dtype)
    return out
```

```python
from contextlib import ExitStack

import concourse.bass as bass
from concourse import mybir

F32 = mybir.dt.float32
ALU = mybir.AluOpType
ACT = mybir.ActivationFunctionType

P = 128
Q = 32
QUADS = P // Q
EPS = 1e-8
DMA = 16

SUM_TAIL, X2_TAIL = 0, 1
X_TRANSPOSE = 0
OUT_TRANSPOSE = 2
XT_COPY = 3
XS_SCALE = 4
OUT_COPY, OUT_FREE = 5, 25
LINEAR = 6
LINEAR_SCALE = 23
SUM_HEAD, X2_HEAD = 24, 25


def build_cond_residual_rnn(nc, x, cond, w0, wx, wh, bias, out):
    B, T, D = x.shape
    HALVES = D // P
    L = P // B
    BLOCKS = T // L
    HL = L // 2
    COLS = HALVES * Q
    assert D == HALVES * P and T == BLOCKS * L and L % 2 == 0 and BLOCKS >= 4

    ctx = ExitStack()
    with ctx:
        def sb(name, shape):
            return ctx.enter_context(nc.sbuf_tensor(name, shape, F32))

        def bank(name):
            return ctx.enter_context(nc.psum_tensor(name, [P, 512], F32))

        def sem(name):
            return ctx.enter_context(nc.semaphore(name))

        w0_sb = sb("w0_sb", [P, HALVES, D])
        wx_sb = sb("wx_sb", [P, HALVES, D])
        wh_sb = sb("wh_sb", [P, HALVES, D])
        w0_sq = sb("w0_sq", [P, HALVES, D])
        bias_sb = sb("bias_sb", [P, D])
        pick_row0 = sb("pick_row0", [P, B])
        ident = sb("ident", [P, P])

        cond_rows = sb("cond_rows", [B, D])
        ys = sb("ys", [P, HALVES, B])
        ys_sq = sb("ys_sq", [P, HALVES, B])
        energy = sb("energy", [P, HALVES, B])
        minus_half = sb("minus_half", [P, HALVES, B])
        demod = sb("demod", [P, HALVES, B])

        tanh_probe = sb("tanh_probe", [1, 1])

        x_rows = sb("x_rows", [P, 2, D])
        x_t = sb("x_t", [P, HALVES, B, L])
        xs_t = sb("xs_t", [P, HALVES, B, L])
        lin_t = sb("lin_t", [P, HALVES, B, L])
        x2_t = sb("x2_t", [P, L, HALVES, B])
        h_t = sb("h_t", [P, L, HALVES, B])
        sum_t = sb("sum_t", [P, HALVES, B, L])
        out_rows = sb("out_rows", [P, D])

        z = [bank("z_even"), bank("z_odd")]
        zt = [bank("zt_half0"), bank("zt_half1")]
        xt_ps = bank("xt_ps")
        lin_ps = bank("lin_ps")
        out_ps = bank("out_ps")
        energy_ps = bank("energy_ps")
        cond_ps = out_ps

        cond_loaded = sem("cond_loaded")
        cond_transposed = sem("cond_transposed")
        w0_loaded = sem("w0_loaded")
        wx_loaded = sem("wx_loaded")
        wh_loaded = sem("wh_loaded")
        bias_zeroed = sem("bias_zeroed")
        bias_loaded = sem("bias_loaded")
        x_first_loaded = sem("x_first_loaded")
        x_loaded = sem("x_loaded")
        zeroed = sem("zeroed")
        pick_set = sem("pick_set")
        ident_zeroed = sem("ident_zeroed")
        ident_ready = sem("ident_ready")
        minus_half_set = sem("minus_half_set")
        tanh_loaded = sem("tanh_loaded")
        ys_ready = sem("ys_ready")
        ys_sq_ready = sem("ys_sq_ready")
        w0_sq_ready = sem("w0_sq_ready")
        energy_summed = sem("energy_summed")
        energy_ready = sem("energy_ready")
        demod_ready = sem("demod_ready")

        z_ready = sem("z_ready")
        zt_ready = [sem("zt0_ready"), sem("zt1_ready")]
        h_ready = [sem("h0_ready"), sem("h1_ready")]
        x_transposed = sem("x_transposed")
        x_t_ready = sem("x_t_ready")
        xs_ready = sem("xs_ready")
        lin_summed = sem("lin_summed")
        lin_ready = sem("lin_ready")
        x2_ready = sem("x2_ready")
        sum_ready = sem("sum_ready")
        out_transposed = sem("out_transposed")
        out_rows_ready = sem("out_rows_ready")
        out_stored = sem("out_stored")

        def blocks(engine, block):
            block(0, True, False)
            with nc.Fori(1, BLOCKS - 1, engines=(engine.engine,), hint_back_edge=True) as i:
                block(i, False, False)
            block(BLOCKS - 1, False, True)

        def token_rows(dram, t0):
            return dram[:, bass.ds(t0, L), :]

        def split_rows(w):
            return w.rearrange("(k p) n -> p k n", p=P)

        block_ctx = ctx.enter_context(nc.Block())

        @block_ctx.sync
        def _(sp):
            sp.dma_start(cond_rows[:], cond).then_inc(cond_loaded, DMA)
            sp.dma_start(x_rows[:, 1, :], token_rows(x, 0)).then_inc(x_first_loaded, DMA)
            sp.dma_start(x_rows[:, 0, :], token_rows(x, L)).then_inc(x_loaded, DMA)
            sp.wait_ge(bias_zeroed, 1)
            sp.dma_start(bias_sb[0:1, :], bias.rearrange("(a n) -> a n", a=1)).then_inc(bias_loaded, DMA)

            def load(i):
                sp.wait_ge(x_transposed, i + 2)
                sp.dma_start(x_rows[:, 0, :], token_rows(x, (i + 2) * L)).then_inc(x_loaded, DMA)

            def store(i):
                sp.wait_ge(out_rows_ready, i + 1)
                sp.dma_start(token_rows(out, i * L), out_rows[:]).then_inc(out_stored, DMA)

            load(0)
            with sp.Fori(1, BLOCKS - 2) as i:
                load(i)
                store(i - 1)
            for i in range(BLOCKS - 3, BLOCKS):
                store(i)
            sp.wait_ge(out_stored, DMA * BLOCKS)

        @block_ctx.gpsimd
        def _(pool):
            nc.gpsimd.memset(minus_half[:], -0.5).then_inc(minus_half_set, 1)
            nc.gpsimd.memset(bias_sb[:], 0.0).then_inc(bias_zeroed, 1)
            nc.gpsimd.memset(ident[:], 0.0).then_inc(ident_zeroed, 1)
            pool.wait_ge(ident_zeroed, 1)
            nc.gpsimd.affine_select(out=ident[:], in_=ident[:], compare_op=ALU.not_equal, fill=1.0,
                                    base=0, pattern=[[-1, P]], channel_multiplier=1).then_inc(ident_ready, 1)
            pool.dma_start(wh_sb[:], split_rows(wh)).then_inc(wh_loaded, DMA)
            pool.wait_ge(minus_half_set, 1)
            pool.wait_ge(energy_ready, 1)
            nc.gpsimd.tensor_tensor(demod[:], energy[:], minus_half[:], ALU.pow).then_inc(demod_ready, 1)

        @block_ctx.tensor
        def _(pe):
            def transpose_x(k, slot):
                return nc.tensor.transpose(xt_ps[:, k * P:(k + 1) * P], x_rows[:, slot, k * P:(k + 1) * P], ident[:])

            def linear(half, b, k):
                at = half * P + b * L
                for q in range(QUADS):
                    rows = slice(Q * q, Q * (q + 1))
                    last = nc.tensor.matmul(lin_ps[rows, at:at + L],
                                            w0_sb[:, k, half * P + Q * q:half * P + Q * (q + 1)], xs_t[:, k, b],
                                            start=(k == 0), stop=(k == HALVES - 1), tile_position=(0, Q * q))
                return last

            def transpose_out(half):
                src = sum_t[:, half].rearrange("p b t -> p (b t)")
                return nc.tensor.transpose(out_ps[:, half * P:(half + 1) * P], src, ident[:])

            def into_z(s, stationary, weights, start=False, stop=False):
                for q in range(QUADS):
                    features = weights.rearrange("p (h q c) -> p q h c", q=QUADS, c=Q)[:, q]
                    last = nc.tensor.matmul(z[s % 2][Q * q:Q * q + B, 0:COLS], stationary, features,
                                            start=start, stop=stop, tile_position=(0, Q * q))
                return last

            def input_part(s):
                into_z(s, pick_row0[:], bias_sb[:], start=True)
                for k in range(HALVES):
                    into_z(s, x2_t[:, s, k], wx_sb[:, k])

            pe.wait_ge(ident_ready, 1)
            pe.wait_ge(cond_loaded, DMA)
            for k in range(HALVES):
                last = nc.tensor.transpose(cond_ps[:, k * B:(k + 1) * B], cond_rows[:, k * P:(k + 1) * P],
                                           ident[0:B, 0:B])
            last.then_inc(cond_transposed, 1)
            pe.wait_ge(x_first_loaded, DMA)
            for k in range(HALVES):
                last = transpose_x(k, 1)
            last.then_inc(x_transposed, 1)

            pe.wait_ge(ys_sq_ready, 1)
            pe.wait_ge(w0_sq_ready, 1)
            for half in range(HALVES):
                for k in range(HALVES):
                    last = nc.tensor.matmul(energy_ps[:, half * B:(half + 1) * B], w0_sq[:, k, half * P:(half + 1) * P],
                                            ys_sq[:, k], start=(k == 0), stop=(k == HALVES - 1))
            last.then_inc(energy_summed, 1)

            pe.wait_ge(xs_ready, 1)
            for half in range(HALVES):
                for k in range(HALVES):
                    last = nc.tensor.matmul(lin_ps[:, half * P:(half + 1) * P], w0_sb[:, k, half * P:(half + 1) * P],
                                            xs_t[:, k].rearrange("p b t -> p (b t)"), start=(k == 0),
                                            stop=(k == HALVES - 1))
            last.then_inc(lin_summed, 1)

            pe.wait_ge(zeroed, 3)
            pe.wait_ge(pick_set, 1)
            pe.wait_ge(bias_loaded, DMA)
            pe.wait_ge(wx_loaded, DMA)
            pe.wait_ge(x2_ready, 1)
            input_part(0)
            pe.wait_ge(wh_loaded, DMA)

            pieces = [(half, b, k) for half in range(HALVES) for b in range(B) for k in range(HALVES)]

            def block(i, first, last_block):
                for s in range(L):
                    pe.wait_ge(h_ready[0], i * L + s + 1)
                    into_z(s, h_t[:, (s - 1) % L, 0], wh_sb[:, 0])
                    pe.wait_ge(h_ready[1], i * L + s + 1)
                    into_z(s, h_t[:, (s - 1) % L, 1], wh_sb[:, 1], stop=True).then_inc(z_ready, 1)

                    if s == HL - 1:
                        pe.wait_ge(x2_ready, 2 * i + 2)
                    if s < L - 1:
                        input_part(s + 1)
                    elif not last_block:
                        pe.wait_ge(x2_ready, 2 * i + 3)
                        input_part(0)

                    if not first and s == OUT_TRANSPOSE:
                        pe.wait_ge(sum_ready, 2 * i)
                        transpose_out(0)
                    if not first and s == OUT_TRANSPOSE + 1:
                        transpose_out(1).then_inc(out_transposed, 1)
                    if last_block:
                        continue
                    if s == X_TRANSPOSE:
                        pe.wait_ge(x_loaded, DMA * (i + 1))
                        transpose_x(0, 0)
                    if s == X_TRANSPOSE + 1:
                        transpose_x(1, 0).then_inc(x_transposed, 1)
                    if s == LINEAR:
                        pe.wait_ge(xs_ready, i + 2)
                    if 0 <= s - LINEAR < len(pieces):
                        last = linear(*pieces[s - LINEAR])
                        if s - LINEAR == len(pieces) - 1:
                            last.then_inc(lin_summed, 1)

            blocks(pe, block)
            pe.wait_ge(sum_ready, 2 * BLOCKS)
            transpose_out(0)
            transpose_out(1).then_inc(out_transposed, 1)

        @block_ctx.vector
        def _(dve):
            def t_last(tile, lo, hi):
                return tile[:].rearrange("p h b t -> p (h b) t")[:, :, lo:hi]

            def t_first(tile, lo, hi):
                return tile[:].rearrange("p t h b -> p (h b) t")[:, :, lo:hi]

            def scale_x(n):
                dve.wait_ge(x_t_ready, n)
                factor = ys[:].rearrange("p h (b o) -> p (h b) o", o=1).broadcast_to([P, HALVES * B, L])
                nc.vector.tensor_tensor(t_last(xs_t, 0, L), t_last(x_t, 0, L), factor, ALU.mult).then_inc(xs_ready, 1)

            def scale_linear(n):
                dve.wait_ge(lin_summed, n)
                factor = demod[:].rearrange("p h (b o) -> p (h b) o", o=1).broadcast_to([P, HALVES * B, L])
                product = lin_ps[:, 0:HALVES * P].rearrange("p (c t) -> p c t", t=L)
                nc.vector.tensor_tensor(t_last(lin_t, 0, L), product, factor, ALU.mult).then_inc(lin_ready, 1)

            def add_x2(lo, hi):
                nc.vector.tensor_tensor(t_first(x2_t, lo, hi), t_last(lin_t, lo, hi), t_last(x_t, lo, hi),
                                        ALU.add).then_inc(x2_ready, 1)

            def add_out(lo, hi):
                nc.vector.tensor_tensor(t_last(sum_t, lo, hi), t_first(x2_t, lo, hi), t_first(h_t, lo, hi),
                                        ALU.add).then_inc(sum_ready, 1)

            nc.vector.memset(pick_row0[:], 0.0).then_inc(zeroed, 1)
            for tile in z:
                nc.vector.memset(tile[:, 0:COLS], 0.0).then_inc(zeroed, 1)
            dve.wait_ge(zeroed, 1)
            nc.vector.memset(pick_row0[0:1, :], 1.0).then_inc(pick_set, 1)

            dve.wait_ge(cond_transposed, 1)
            nc.vector.tensor_scalar(ys[:].rearrange("p h b -> p (h b)"), cond_ps[:, 0:HALVES * B], float(D) ** -0.5,
                                    None, ALU.mult).then_inc(ys_ready, 1)
            dve.wait_ge(ys_ready, 1)
            nc.vector.tensor_tensor(ys_sq[:], ys[:], ys[:], ALU.mult).then_inc(ys_sq_ready, 1)
            for half in range(HALVES):
                nc.vector.tensor_copy(h_t[:, L - 1, half], cond_ps[:, half * B:(half + 1) * B])\
                    .then_inc(h_ready[half], 1)
            dve.wait_ge(w0_loaded, DMA)
            nc.vector.tensor_tensor(w0_sq[:], w0_sb[:], w0_sb[:], ALU.mult).then_inc(w0_sq_ready, 1)
            scale_x(1)
            dve.wait_ge(energy_summed, 1)
            nc.vector.tensor_scalar(energy[:].rearrange("p h b -> p (h b)"), energy_ps[:, 0:HALVES * B], EPS, None,
                                    ALU.add).then_inc(energy_ready, 1)
            dve.wait_ge(demod_ready, 1)
            scale_linear(1)
            dve.wait_ge(lin_ready, 1)
            add_x2(0, HL)
            add_x2(HL, L)

            def block(i, first, last_block):
                for s in range(L):
                    dve.wait_ge(z_ready, i * L + s + 1)
                    for half in range(HALVES):
                        nc.vector.transpose(zt[half][:, 0:Q], z[s % 2][:, half * Q:(half + 1) * Q])\
                            .then_inc(zt_ready[half], 1)

                    if not first and s == SUM_TAIL:
                        add_out(HL, L)
                    if not first and s == X2_TAIL:
                        dve.wait_ge(sum_ready, 2 * i)
                        add_x2(HL, L)
                    if s == SUM_HEAD:
                        add_out(0, HL)
                    if last_block:
                        continue
                    if s == XS_SCALE:
                        scale_x(i + 2)
                    if s == LINEAR_SCALE:
                        scale_linear(i + 2)
                    if s == X2_HEAD:
                        dve.wait_ge(lin_ready, i + 2)
                        dve.wait_ge(sum_ready, 2 * i + 1)
                        add_x2(0, HL)

            blocks(dve, block)
            for ready in h_ready:
                dve.wait_ge(ready, T + 1)
            add_out(HL, L)

        @block_ctx.scalar
        def _(act):
            act.dma_start(w0_sb[:], split_rows(w0)).then_inc(w0_loaded, DMA)
            act.dma_start(wx_sb[:], split_rows(wx)).then_inc(wx_loaded, DMA)
            act.wait_ge(minus_half_set, 1)
            nc.scalar.activation(tanh_probe[:], minus_half[0:1, 0, 0:1], ACT.Tanh).then_inc(tanh_loaded, 1)

            def copy_x(n):
                act.wait_ge(x_transposed, n)
                nc.scalar.copy(x_t[:].rearrange("p h b t -> p (h b t)"), xt_ps[:, 0:HALVES * P]).then_inc(x_t_ready, 1)

            def copy_out(n):
                act.wait_ge(out_transposed, n)
                nc.scalar.copy(out_rows[:], out_ps[:, 0:D]).then_inc(out_rows_ready, 1)

            copy_x(1)

            def block(i, first, last_block):
                for s in range(L):
                    for half in range(HALVES):
                        act.wait_ge(zt_ready[half], i * L + s + 1)
                        nc.scalar.activation(h_t[:, s, half], zt[half][:, 0:B], ACT.Tanh).then_inc(h_ready[half], 1)
                    if not first and s == OUT_COPY:
                        copy_out(i)
                    if not first and s == OUT_FREE:
                        act.wait_ge(out_stored, DMA * i)
                    if not last_block and s == XT_COPY:
                        copy_x(i + 2)

            blocks(act, block)
            copy_out(BLOCKS)


_INS = ["x", "cond_1024", "L0_cond_weight", "L1_cond_Wx", "L1_cond_Wh", "L1_cond_b"]
_OUTS = [((4, 512, 256), "float32")]


def kernel(**inputs):
    import numpy as _np
    import concourse.bacc as _bacc
    from concourse import mybir as _mybir
    from concourse.bass_utils import run_bass_kernel_spmd as _run

    nc = _bacc.Bacc("TRN2", target_bir_lowering=False, num_devices=1)
    arrays, args = {}, []
    for name in _INS:
        a = _np.ascontiguousarray(inputs[name])
        arrays[f"in_{name}_dram"] = a
        args.append(nc.dram_tensor(f"in_{name}_dram", a.shape, _mybir.dt.from_np(a.dtype), kind="ExternalInput").ap())
    for i, (shape, dtype) in enumerate(_OUTS):
        dt = _mybir.dt.from_np(_np.dtype(dtype))
        args.append(nc.dram_tensor(f"out_{i}_dram", shape, dt, kind="ExternalOutput").ap())
    build_cond_residual_rnn(nc, *args)
    r = _run(nc, [arrays], core_ids=[0])
    return r.results[0]["out_0_dram"]
```

```python
from contextlib import ExitStack

import concourse.bass as bass
from concourse import mybir

F32 = mybir.dt.float32
BF16 = mybir.dt.bfloat16
ALU = mybir.AluOpType
ACT = mybir.ActivationFunctionType

P = 128
Q = 32
QUADS = P // Q
BANK = 512
EPS = 1e-8
DMA = 16
WINDOW = 7

FILL_EVEN, FILL_ODD, FILL_PIECE, FILL_TRANSPOSES = 640, 352, 32, 96

X_TRANSPOSE = 0
X_COPY = 1
LINEAR = (4, 6, 8, 10)
OUT_TRANSPOSE = 14
OUT_COPY, OUT_FREE = 15, 30
INPUT = (16, 18, 20, 22)
SEED_TAIL = (1, 2)
SEED_HEAD = (27, 28)


def build_cond_residual_rnn(nc, x, cond, w0, wx, wh, bias, out):
    B, T, D = x.shape
    HALVES = D // P
    L = P // B
    BLOCKS = T // L
    HL = L // 2
    PAD = (WINDOW - 1) * B
    SLOTS = L // 2
    assert HALVES == 2 and D == HALVES * P and T == BLOCKS * L and L % 4 == 0 and BLOCKS >= 4
    assert SEED_HEAD[0] // 2 + 1 - (WINDOW - 1) >= SLOTS // 2

    ctx = ExitStack()
    with ctx:
        def sb(name, shape, dtype=F32):
            return ctx.enter_context(nc.sbuf_tensor(name, shape, dtype))

        def bank(name):
            return ctx.enter_context(nc.psum_tensor(name, [P, BANK], F32))

        def sem(name):
            return ctx.enter_context(nc.semaphore(name))

        w0_sb = sb("w0_sb", [P, HALVES, D])
        wx_sb = sb("wx_sb", [P, HALVES, D])
        wh_sb = sb("wh_sb", [P, HALVES, D])
        w0_sq = sb("w0_sq", [P, HALVES, D])
        bias_rows = sb("bias_rows", [HALVES, P])
        bias_t = sb("bias_t", [P, HALVES])
        ident = sb("ident", [P, P])
        zeros = sb("zeros", [P, BANK], BF16)

        cond_rows = sb("cond_rows", [B, D])
        ys = sb("ys", [P, HALVES, B])
        ys_sq = sb("ys_sq", [P, HALVES, B])
        energy = sb("energy", [P, HALVES, B])
        minus_half = sb("minus_half", [P, HALVES, B])
        demod = sb("demod", [P, HALVES, B])
        tanh_probe = sb("tanh_probe", [1, 1])

        x_rows = sb("x_rows", [P, 2, D])
        x_t = sb("x_t", [P, HALVES, B, L])
        xs_t = sb("xs_t", [P, HALVES, B, L])
        lin_t = sb("lin_t", [P, HALVES, B, L])
        x2_next = sb("x2_next", [P, HALVES, B, L])
        x2_now = sb("x2_now", [P, HALVES, B, L])
        h_t = sb("h_t", [P, HALVES, PAD + L * B])
        sum_t = sb("sum_t", [P, HALVES, B, L])
        out_rows = sb("out_rows", [P, D])

        z = [[bank(f"z{half}_{parity}") for parity in ("even", "odd")] for half in range(HALVES)]
        rows_ps = bank("rows_ps")
        lin_ps = bank("lin_ps")
        input_ps = bank("input_ps")
        idle_ps = bank("idle_ps")
        xt_ps, out_ps = rows_ps[:, 0:D], rows_ps[:, D:2 * D]
        cond_ps = lin_ps[:, 0:HALVES * B]
        bias_ps = lin_ps[:, HALVES * B:HALVES * (B + 1)]
        energy_ps = input_ps[:, 0:HALVES * B]

        cond_loaded = sem("cond_loaded")
        w0_loaded = sem("w0_loaded")
        wx_loaded = sem("wx_loaded")
        wh_loaded = sem("wh_loaded")
        bias_loaded = sem("bias_loaded")
        x_first_loaded = sem("x_first_loaded")
        x_loaded = sem("x_loaded")
        zeros_set = sem("zeros_set")
        h_padded = sem("h_padded")
        ident_zeroed = sem("ident_zeroed")
        ident_ready = sem("ident_ready")
        minus_half_set = sem("minus_half_set")
        tanh_loaded = sem("tanh_loaded")
        cond_transposed = sem("cond_transposed")
        bias_ready = sem("bias_ready")
        ys_ready = sem("ys_ready")
        ys_sq_ready = sem("ys_sq_ready")
        w0_sq_ready = sem("w0_sq_ready")
        energy_summed = sem("energy_summed")
        energy_ready = sem("energy_ready")
        demod_ready = sem("demod_ready")
        z_opened = sem("z_opened")

        z_ready = [sem("z0_ready"), sem("z1_ready")]
        h_ready = [sem("h0_ready"), sem("h1_ready")]
        z_seeded = sem("z_seeded")
        x_transposed = sem("x_transposed")
        x_t_ready = sem("x_t_ready")
        xs_ready = sem("xs_ready")
        lin_summed = sem("lin_summed")
        lin_ready = sem("lin_ready")
        x2_ready = sem("x2_ready")
        x2_kept = sem("x2_kept")
        input_summed = sem("input_summed")
        sum_ready = sem("sum_ready")
        out_transposed = sem("out_transposed")
        out_rows_ready = sem("out_rows_ready")
        out_stored = sem("out_stored")

        assert X_TRANSPOSE < LINEAR[0] and LINEAR[-1] < OUT_TRANSPOSE < INPUT[0] and INPUT[-1] < SEED_HEAD[0]

        def blocks(engine, block):
            block(0, True, False)
            with nc.Fori(1, BLOCKS - 1, engines=(engine.engine,), hint_back_edge=True) as i:
                block(i, False, False)
            block(BLOCKS - 1, False, True)

        def token_rows(dram, t0):
            return dram[:, bass.ds(t0, L), :]

        def split_rows(w):
            return w.rearrange("(k p) n -> p k n", p=P)

        block_ctx = ctx.enter_context(nc.Block())

        @block_ctx.sync
        def _(sp):
            sp.dma_start(cond_rows[:], cond).then_inc(cond_loaded, DMA)
            sp.dma_start(x_rows[:, 1, :], token_rows(x, 0)).then_inc(x_first_loaded, DMA)
            sp.dma_start(bias_rows[:], bias.rearrange("(h p) -> h p", p=P)).then_inc(bias_loaded, DMA)
            sp.dma_start(x_rows[:, 0, :], token_rows(x, L)).then_inc(x_loaded, DMA)

            def load(i):
                sp.wait_ge(x_transposed, i + 2)
                sp.dma_start(x_rows[:, 0, :], token_rows(x, (i + 2) * L)).then_inc(x_loaded, DMA)

            def store(i):
                sp.wait_ge(out_rows_ready, i + 1)
                sp.dma_start(token_rows(out, i * L), out_rows[:]).then_inc(out_stored, DMA)

            load(0)
            with sp.Fori(1, BLOCKS - 2) as i:
                load(i)
                store(i - 1)
            for i in range(BLOCKS - 3, BLOCKS):
                store(i)
            sp.wait_ge(out_stored, DMA * BLOCKS)

        @block_ctx.gpsimd
        def _(pool):
            nc.gpsimd.memset(ident[:], 0.0).then_inc(ident_zeroed, 1)
            nc.gpsimd.memset(minus_half[:], -0.5).then_inc(minus_half_set, 1)
            pool.wait_ge(ident_zeroed, 1)
            nc.gpsimd.affine_select(out=ident[:], in_=ident[:], compare_op=ALU.not_equal, fill=1.0,
                                    base=0, pattern=[[-1, P]], channel_multiplier=1).then_inc(ident_ready, 1)
            nc.gpsimd.memset(h_t[:, :, 0:PAD], 0.0).then_inc(h_padded, 1)
            nc.gpsimd.memset(h_t[:, :, (L - 1) * B:PAD + (L - 1) * B], 0.0).then_inc(h_padded, 1)
            pool.dma_start(wh_sb[:], split_rows(wh)).then_inc(wh_loaded, DMA)
            pool.wait_ge(minus_half_set, 1)
            pool.wait_ge(energy_ready, 1)
            nc.gpsimd.tensor_tensor(demod[:], energy[:], minus_half[:], ALU.pow).then_inc(demod_ready, 1)

        @block_ctx.tensor
        def _(pe):
            def stream_zeros(columns):
                while columns > 0:
                    n = min(columns, BANK)
                    nc.tensor.matmul(idle_ps[0:Q, 0:n], zeros[:, 0:Q], zeros[:, 0:n], start=True, stop=True,
                                     tile_position=(0, 0))
                    columns -= n

            def transpose_x(slot):
                for k in range(HALVES):
                    last = nc.tensor.transpose(xt_ps[:, k * P:(k + 1) * P], x_rows[:, slot, k * P:(k + 1) * P],
                                               ident[:])
                last.then_inc(x_transposed, 1)

            def transpose_out():
                for half in range(HALVES):
                    last = nc.tensor.transpose(out_ps[:, half * P:(half + 1) * P],
                                               sum_t[:, half].rearrange("p b t -> p (b t)"), ident[:])
                last.then_inc(out_transposed, 1)

            def by_tiles(dst, weights, half, moving, **flags):
                for q in range(QUADS):
                    at = half * P + Q * q
                    last = nc.tensor.matmul(dst[Q * q:Q * (q + 1), :], weights[:, at:at + Q], moving,
                                            tile_position=(0, Q * q), **flags)
                return last

            PIECES = [(half, k) for half in range(HALVES) for k in range(HALVES)]

            def piece_of_product(dst, weights, tokens, half, k):
                return by_tiles(dst[:, half * P:(half + 1) * P], weights[:, k], half,
                                tokens[:, k].rearrange("p b t -> p (b t)"), start=(k == 0), stop=(k == HALVES - 1))

            def whole_product(dst, weights, tokens):
                for half, k in PIECES:
                    last = piece_of_product(dst, weights, tokens, half, k)
                return last

            pe.wait_ge(zeros_set, 1)
            for half in range(HALVES):
                for parity in range(2):
                    for q in range(QUADS):
                        last = nc.tensor.matmul(z[half][parity][Q * q:Q * (q + 1), 0:PAD + SLOTS * B], zeros[:, 0:Q],
                                                zeros[:, 0:PAD + SLOTS * B], start=True, stop=True,
                                                tile_position=(0, Q * q))
            last.then_inc(z_opened, 1)

            stream_zeros(1280)
            pe.wait_ge(ident_ready, 1)
            pe.wait_ge(cond_loaded, DMA)
            for k in range(HALVES):
                last = nc.tensor.transpose(cond_ps[:, k * B:(k + 1) * B], cond_rows[:, k * P:(k + 1) * P],
                                           ident[0:B, 0:B])
            last.then_inc(cond_transposed, 1)
            stream_zeros(1408)
            pe.wait_ge(x_first_loaded, DMA)
            transpose_x(1)

            stream_zeros(640)
            pe.wait_ge(ys_sq_ready, 1)
            pe.wait_ge(w0_sq_ready, 1)
            for half in range(HALVES):
                for k in range(HALVES):
                    last = by_tiles(energy_ps[:, half * B:(half + 1) * B], w0_sq[:, k], half, ys_sq[:, k],
                                    start=(k == 0), stop=(k == HALVES - 1))
            last.then_inc(energy_summed, 1)
            pe.wait_ge(bias_loaded, DMA)
            nc.tensor.transpose(bias_ps, bias_rows[:], ident[0:HALVES, 0:HALVES]).then_inc(cond_transposed, 1)

            stream_zeros(512)
            pe.wait_ge(bias_ready, 1)
            pe.wait_ge(xs_ready, 1)
            whole_product(lin_ps, w0_sb, xs_t).then_inc(lin_summed, 1)
            stream_zeros(6144)
            pe.wait_ge(wx_loaded, DMA)
            pe.wait_ge(x2_ready, 1)
            whole_product(input_ps, wx_sb, x2_next).then_inc(input_summed, 1)
            pe.wait_ge(wh_loaded, DMA)
            pe.wait_ge(h_padded, 2)
            stream_zeros(1536)
            pe.wait_ge(z_seeded, 2)

            ORDERS = ([(0, 0), (0, 1), (1, 0), (1, 1)], [(0, 0), (1, 0), (0, 1), (1, 1)])

            def block(i, first, last_block):
                for s in range(L):
                    if s in (SEED_TAIL[0] + 1, SEED_TAIL[1] + 1):
                        pe.wait_ge(z_seeded, 4 * i + 3 + SEED_TAIL.index(s - 1))
                    if not last_block and s in (SEED_HEAD[0] + 1, SEED_HEAD[1] + 1):
                        pe.wait_ge(z_seeded, 4 * i + 5 + SEED_HEAD.index(s - 1))

                    h_end = PAD + B * ((s - 1) % L + 1)
                    z_end = PAD + B * (s // 2 + 1)
                    waited = set()
                    for k, half in ORDERS[s % 2]:
                        if k not in waited:
                            pe.wait_ge(h_ready[k], i * L + s + 1)
                            waited.add(k)
                        last = by_tiles(z[half][s % 2][:, z_end - WINDOW * B:z_end], wh_sb[:, k], half,
                                        h_t[:, k, h_end - WINDOW * B:h_end], start=False, stop=True,
                                        skip_group_check=True)
                        if k == HALVES - 1:
                            last.then_inc(z_ready[half], 1)

                    if last_block and s == L - 1:
                        continue
                    fill = FILL_EVEN if s % 2 == 0 else FILL_ODD
                    if not last_block:
                        if s == X_TRANSPOSE:
                            pe.wait_ge(x_loaded, DMA * (i + 1))
                            transpose_x(0)
                            fill = FILL_TRANSPOSES
                        if s == LINEAR[0]:
                            pe.wait_ge(xs_ready, i + 2)
                        if s == INPUT[0]:
                            pe.wait_ge(x2_ready, i + 2)
                        if s in LINEAR:
                            last = piece_of_product(lin_ps, w0_sb, xs_t, *PIECES[LINEAR.index(s)])
                            fill = FILL_PIECE
                        if s in INPUT:
                            last = piece_of_product(input_ps, wx_sb, x2_next, *PIECES[INPUT.index(s)])
                            fill = FILL_PIECE
                        if s == LINEAR[-1]:
                            last.then_inc(lin_summed, 1)
                        if s == INPUT[-1]:
                            last.then_inc(input_summed, 1)
                    if not first and s == OUT_TRANSPOSE:
                        pe.wait_ge(sum_ready, 2 * i)
                        transpose_out()
                        fill = FILL_TRANSPOSES
                    stream_zeros(fill)

            blocks(pe, block)
            pe.wait_ge(sum_ready, 2 * BLOCKS)
            transpose_out()

        @block_ctx.vector
        def _(dve):
            def cut(tile, lo, hi):
                return tile[:].rearrange("p h b t -> p (h b) t")[:, :, lo:hi]

            def per_column(tile):
                return tile[:].rearrange("p h (b o) -> p (h b) o", o=1).broadcast_to([P, HALVES * B, L])

            def scale_x(n):
                dve.wait_ge(x_t_ready, n)
                nc.vector.tensor_tensor(cut(xs_t, 0, L), cut(x_t, 0, L), per_column(ys), ALU.mult)\
                    .then_inc(xs_ready, 1)

            def make_x2(n):
                dve.wait_ge(lin_summed, n)
                product = lin_ps[:, 0:D].rearrange("p (c t) -> p c t", t=L)
                nc.vector.tensor_tensor(cut(lin_t, 0, L), product, per_column(demod), ALU.mult).then_inc(lin_ready, 1)
                dve.wait_ge(lin_ready, n)
                nc.vector.tensor_tensor(cut(x2_next, 0, L), cut(lin_t, 0, L), cut(x_t, 0, L), ALU.add)\
                    .then_inc(x2_ready, 1)

            def keep_x2(lo, hi):
                nc.vector.tensor_copy(cut(x2_now, lo, hi), cut(x2_next, lo, hi)).then_inc(x2_kept, 1)

            def add_out(lo, hi):
                for half in range(HALVES):
                    h = h_t[:, half, PAD + B * lo:PAD + B * hi].rearrange("p (t b) -> p b t", b=B)
                    last = nc.vector.tensor_tensor(sum_t[:, half, :, lo:hi], x2_now[:, half, :, lo:hi], h, ALU.add)
                last.then_inc(sum_ready, 1)

            def seed(parity, lo, hi):
                for half in range(HALVES):
                    src = input_ps[:, half * P:(half + 1) * P].rearrange("p (b u v) -> p v u b", b=B, v=2)
                    dst = z[half][parity][:, PAD + B * lo // 2:PAD + B * hi // 2].rearrange("p (u b) -> p u b", b=B)
                    last = nc.vector.tensor_scalar(dst, src[:, parity, lo // 2:hi // 2], bias_t[:, half:half + 1],
                                                   None, ALU.add)
                last.then_inc(z_seeded, 1)

            def states_written(count):
                for ready in h_ready:
                    dve.wait_ge(ready, count)

            nc.vector.memset(zeros[:], 0.0).then_inc(zeros_set, 1)
            dve.wait_ge(cond_transposed, 1)
            nc.vector.tensor_scalar(ys[:].rearrange("p h b -> p (h b)"), cond_ps, float(D) ** -0.5,
                                    None, ALU.mult).then_inc(ys_ready, 1)
            dve.wait_ge(ys_ready, 1)
            nc.vector.tensor_tensor(ys_sq[:], ys[:], ys[:], ALU.mult).then_inc(ys_sq_ready, 1)
            for half in range(HALVES):
                nc.vector.tensor_copy(h_t[:, half, PAD + B * (L - 1):PAD + B * L],
                                      cond_ps[:, half * B:(half + 1) * B]).then_inc(h_ready[half], 1)
            dve.wait_ge(w0_loaded, DMA)
            nc.vector.tensor_tensor(w0_sq[:], w0_sb[:], w0_sb[:], ALU.mult).then_inc(w0_sq_ready, 1)
            scale_x(1)
            dve.wait_ge(energy_summed, 1)
            nc.vector.tensor_scalar(energy[:].rearrange("p h b -> p (h b)"), energy_ps, EPS, None,
                                    ALU.add).then_inc(energy_ready, 1)
            dve.wait_ge(cond_transposed, 2)
            nc.vector.tensor_copy(bias_t[:], bias_ps).then_inc(bias_ready, 1)
            dve.wait_ge(demod_ready, 1)
            make_x2(1)
            dve.wait_ge(x2_ready, 1)
            keep_x2(0, HL)
            keep_x2(HL, L)
            dve.wait_ge(z_opened, 1)
            dve.wait_ge(input_summed, 1)
            dve.wait_ge(bias_ready, 1)
            for parity in range(2):
                seed(parity, 0, HL)

            def block(i, first, last_block):
                if not first:
                    states_written(i * L + 1)
                    dve.wait_ge(x2_kept, 2 * i + 1)
                    add_out(HL, L)
                for parity, s in enumerate(SEED_TAIL):
                    states_written(i * L + s + 1)
                    seed(parity, HL, L)
                if not first:
                    dve.wait_ge(sum_ready, 2 * i)
                    keep_x2(HL, L)
                if not last_block:
                    scale_x(i + 2)
                    dve.wait_ge(x2_kept, 2 * i + 2)
                    make_x2(i + 2)
                states_written(i * L + HL + 1)
                if not first:
                    dve.wait_ge(out_transposed, i)
                add_out(0, HL)
                if not last_block:
                    dve.wait_ge(x2_ready, i + 2)
                    dve.wait_ge(sum_ready, 2 * i + 1)
                    keep_x2(0, HL)
                    dve.wait_ge(input_summed, i + 2)
                    for parity, s in enumerate(SEED_HEAD):
                        states_written(i * L + s + 1)
                        seed(parity, 0, HL)

            blocks(dve, block)
            states_written(T + 1)
            dve.wait_ge(x2_kept, 2 * BLOCKS)
            add_out(HL, L)

        @block_ctx.scalar
        def _(act):
            act.dma_start(w0_sb[:], split_rows(w0)).then_inc(w0_loaded, DMA)
            act.dma_start(wx_sb[:], split_rows(wx)).then_inc(wx_loaded, DMA)
            act.wait_ge(minus_half_set, 1)
            nc.scalar.activation(tanh_probe[:], minus_half[0:1, 0, 0:1], ACT.Tanh).then_inc(tanh_loaded, 1)

            def copy_x(n):
                act.wait_ge(x_transposed, n)
                nc.scalar.copy(x_t[:].rearrange("p h b t -> p (h b t)"), xt_ps).then_inc(x_t_ready, 1)

            def copy_out(n):
                act.wait_ge(out_transposed, n)
                nc.scalar.copy(out_rows[:], out_ps).then_inc(out_rows_ready, 1)

            copy_x(1)

            def block(i, first, last_block):
                for s in range(L):
                    h_at, z_at = PAD + B * s, PAD + B * (s // 2)
                    for half in range(HALVES):
                        act.wait_ge(z_ready[half], i * L + s + 1)
                        nc.scalar.activation(h_t[:, half, h_at:h_at + B], z[half][s % 2][:, z_at:z_at + B],
                                             ACT.Tanh).then_inc(h_ready[half], 1)
                    if not last_block and s == X_COPY:
                        copy_x(i + 2)
                    if not first and s == OUT_COPY:
                        copy_out(i)
                    if not first and s == OUT_FREE:
                        act.wait_ge(out_stored, DMA * i)

            blocks(act, block)
            copy_out(BLOCKS)


_INS = ["x", "cond_1024", "L0_cond_weight", "L1_cond_Wx", "L1_cond_Wh", "L1_cond_b"]
_OUTS = [((4, 512, 256), "float32")]


def kernel(**inputs):
    import numpy as _np
    import concourse.bacc as _bacc
    from concourse import mybir as _mybir
    from concourse.bass_utils import run_bass_kernel_spmd as _run

    nc = _bacc.Bacc("TRN2", target_bir_lowering=False, num_devices=1)
    arrays, args = {}, []
    for name in _INS:
        a = _np.ascontiguousarray(inputs[name])
        arrays[f"in_{name}_dram"] = a
        args.append(nc.dram_tensor(f"in_{name}_dram", a.shape, _mybir.dt.from_np(a.dtype), kind="ExternalInput").ap())
    for i, (shape, dtype) in enumerate(_OUTS):
        dt = _mybir.dt.from_np(_np.dtype(dtype))
        args.append(nc.dram_tensor(f"out_{i}_dram", shape, dt, kind="ExternalOutput").ap())
    build_cond_residual_rnn(nc, *args)
    r = _run(nc, [arrays], core_ids=[0])
    return r.results[0]["out_0_dram"]
```

```python
from contextlib import ExitStack

import concourse.bass as bass
from concourse import mybir

F32 = mybir.dt.float32
BF16 = mybir.dt.bfloat16
ALU = mybir.AluOpType
ACT = mybir.ActivationFunctionType

P = 128
Q = 32
QUADS = P // Q
BANK = 512
EPS = 1e-8
DMA = 16
WINDOW = 7

FILL_EVEN, FILL_ODD, FILL_TRANSPOSES = 672, 352, 96

X_TRANSPOSE = 0
X_COPY = 1
LINEAR = (4, 6, 8, 10)
OUT_TRANSPOSE = 14
OUT_COPY, OUT_FREE = 15, 30
INPUT = (16, 18, 20, 22)
SEED_TAIL = (1, 2)
SEED_HEAD = (27, 28)


def build_cond_residual_rnn(nc, x, cond, w0, wx, wh, bias, out):
    B, T, D = x.shape
    HALVES = D // P
    L = P // B
    BLOCKS = T // L
    HL = L // 2
    PAD = (WINDOW - 1) * B
    SLOTS = L // 2
    assert HALVES == 2 and D == HALVES * P and T == BLOCKS * L and L % 4 == 0 and BLOCKS >= 4
    assert SEED_HEAD[0] // 2 + 1 - (WINDOW - 1) >= SLOTS // 2

    ctx = ExitStack()
    with ctx:
        def sb(name, shape, dtype=F32):
            return ctx.enter_context(nc.sbuf_tensor(name, shape, dtype))

        def bank(name):
            return ctx.enter_context(nc.psum_tensor(name, [P, BANK], F32))

        def sem(name):
            return ctx.enter_context(nc.semaphore(name))

        w0_sb = sb("w0_sb", [P, HALVES, D])
        wx_sb = sb("wx_sb", [P, HALVES, D])
        wh_sb = sb("wh_sb", [P, HALVES, D])
        w0_sq = sb("w0_sq", [P, HALVES, D])
        bias_t = sb("bias_t", [P, HALVES])
        ident = sb("ident", [P, P])
        zeros = sb("zeros", [P, BANK], BF16)

        cond_rows = sb("cond_rows", [B, D])
        ys = sb("ys", [P, HALVES, B])
        ys_sq = sb("ys_sq", [P, HALVES, B])
        energy = sb("energy", [P, HALVES, B])
        minus_half = sb("minus_half", [P, HALVES, B])
        demod = sb("demod", [P, HALVES, B])
        tanh_probe = sb("tanh_probe", [1, 1])

        x_rows = sb("x_rows", [P, 2, D])
        x_t = sb("x_t", [P, HALVES, B, L])
        xs_t = sb("xs_t", [P, HALVES, B, L])
        lin_t = sb("lin_t", [P, HALVES, B, L])
        x2_next = sb("x2_next", [P, HALVES, B, L])
        x2_now = sb("x2_now", [P, HALVES, B, L])
        h_t = sb("h_t", [P, HALVES, PAD + L * B])
        sum_t = sb("sum_t", [P, HALVES, B, L])
        out_rows = sb("out_rows", [P, D])

        z = [[bank(f"z{half}_{parity}") for parity in ("even", "odd")] for half in range(HALVES)]
        rows_ps = bank("rows_ps")
        lin_ps = bank("lin_ps")
        input_ps = bank("input_ps")
        idle_ps = bank("idle_ps")
        xt_ps, out_ps = rows_ps[:, 0:D], rows_ps[:, D:2 * D]
        last_ps = [out_ps, lin_ps]
        cond_ps = lin_ps[:, 0:HALVES * B]
        energy_ps = input_ps[:, 0:HALVES * B]

        cond_loaded = sem("cond_loaded")
        w0_loaded = sem("w0_loaded")
        wx_loaded = sem("wx_loaded")
        wh_loaded = sem("wh_loaded")
        bias_loaded = sem("bias_loaded")
        x_first_loaded = sem("x_first_loaded")
        x_loaded = sem("x_loaded")
        zeros_set = sem("zeros_set")
        h_padded = sem("h_padded")
        ident_zeroed = sem("ident_zeroed")
        ident_ready = sem("ident_ready")
        minus_half_set = sem("minus_half_set")
        tanh_loaded = sem("tanh_loaded")
        cond_transposed = sem("cond_transposed")
        ys_ready = sem("ys_ready")
        ys_sq_ready = sem("ys_sq_ready")
        w0_sq_ready = sem("w0_sq_ready")
        energy_summed = sem("energy_summed")
        energy_ready = sem("energy_ready")
        demod_ready = sem("demod_ready")
        z_opened = sem("z_opened")

        z_ready = [sem("z0_ready"), sem("z1_ready")]
        h_ready = [sem("h0_ready"), sem("h1_ready")]
        z_seeded = sem("z_seeded")
        x_transposed = sem("x_transposed")
        x_t_ready = sem("x_t_ready")
        xs_ready = sem("xs_ready")
        lin_summed = sem("lin_summed")
        lin_ready = sem("lin_ready")
        x2_ready = sem("x2_ready")
        x2_kept = sem("x2_kept")
        input_summed = sem("input_summed")
        sum_ready = sem("sum_ready")
        out_transposed = sem("out_transposed")
        out_rows_ready = sem("out_rows_ready")
        out_stored = sem("out_stored")

        assert X_TRANSPOSE < LINEAR[0] and LINEAR[-1] < OUT_TRANSPOSE < INPUT[0] and INPUT[-1] < SEED_HEAD[0]

        def blocks(engine, block):
            block(0, True, False)
            with nc.Fori(1, BLOCKS - 1, engines=(engine.engine,), hint_back_edge=True) as i:
                block(i, False, False)
            block(BLOCKS - 1, False, True)

        def token_rows(dram, t0):
            return dram[:, bass.ds(t0, L), :]

        def split_rows(w):
            return w.rearrange("(k p) n -> p k n", p=P)

        block_ctx = ctx.enter_context(nc.Block())

        @block_ctx.sync
        def _(sp):
            sp.dma_start(cond_rows[:], cond).then_inc(cond_loaded, DMA)
            sp.dma_start(x_rows[:, 1, :], token_rows(x, 0)).then_inc(x_first_loaded, DMA)
            sp.dma_start(bias_t[:], bias.rearrange("(h p) -> p h", p=P), allow_slow_non_contiguous=True)\
                .then_inc(bias_loaded, DMA)
            sp.dma_start(x_rows[:, 0, :], token_rows(x, L)).then_inc(x_loaded, DMA)

            def load(i):
                sp.wait_ge(x_transposed, i + 2)
                sp.dma_start(x_rows[:, 0, :], token_rows(x, (i + 2) * L)).then_inc(x_loaded, DMA)

            def store(i):
                sp.wait_ge(out_rows_ready, i + 1)
                sp.dma_start(token_rows(out, i * L), out_rows[:]).then_inc(out_stored, DMA)

            load(0)
            with sp.Fori(1, BLOCKS - 2) as i:
                load(i)
                store(i - 1)
            store(BLOCKS - 3)
            store(BLOCKS - 2)
            sp.wait_ge(out_rows_ready, BLOCKS + 1)
            sp.dma_start(token_rows(out, (BLOCKS - 1) * L), out_rows[:]).then_inc(out_stored, DMA)
            sp.wait_ge(out_stored, DMA * BLOCKS)

        @block_ctx.gpsimd
        def _(pool):
            nc.gpsimd.memset(ident[:], 0.0).then_inc(ident_zeroed, 1)
            nc.gpsimd.memset(minus_half[:], -0.5).then_inc(minus_half_set, 1)
            pool.wait_ge(ident_zeroed, 1)
            nc.gpsimd.affine_select(out=ident[:], in_=ident[:], compare_op=ALU.not_equal, fill=1.0,
                                    base=0, pattern=[[-1, P]], channel_multiplier=1).then_inc(ident_ready, 1)
            nc.gpsimd.memset(h_t[:, :, 0:PAD], 0.0).then_inc(h_padded, 1)
            nc.gpsimd.memset(h_t[:, :, (L - 1) * B:PAD + (L - 1) * B], 0.0).then_inc(h_padded, 1)
            pool.dma_start(wh_sb[:], split_rows(wh)).then_inc(wh_loaded, DMA)
            pool.wait_ge(minus_half_set, 1)
            pool.wait_ge(energy_ready, 1)
            nc.gpsimd.tensor_tensor(demod[:], energy[:], minus_half[:], ALU.pow).then_inc(demod_ready, 1)

        @block_ctx.tensor
        def _(pe):
            def stream_zeros(columns):
                while columns > 0:
                    n = min(columns, BANK)
                    nc.tensor.matmul(idle_ps[0:Q, 0:n], zeros[:, 0:Q], zeros[:, 0:n], start=True, stop=True,
                                     tile_position=(0, 0))
                    columns -= n

            def transpose_x(slot):
                for k in range(HALVES):
                    last = nc.tensor.transpose(xt_ps[:, k * P:(k + 1) * P], x_rows[:, slot, k * P:(k + 1) * P],
                                               ident[:])
                last.then_inc(x_transposed, 1)

            def transpose_half(dst, half):
                return nc.tensor.transpose(dst[:, half * P:(half + 1) * P],
                                           sum_t[:, half].rearrange("p b t -> p (b t)"), ident[:])

            def transpose_out():
                for half in range(HALVES):
                    last = transpose_half(out_ps, half)
                last.then_inc(out_transposed, 1)

            def by_tiles(dst, weights, half, moving, **flags):
                for q in range(QUADS):
                    at = half * P + Q * q
                    last = nc.tensor.matmul(dst[Q * q:Q * (q + 1), :], weights[:, at:at + Q], moving,
                                            tile_position=(0, Q * q), **flags)
                return last

            PIECES = [(half, k) for half in range(HALVES) for k in range(HALVES)]

            def piece_of_product(dst, weights, tokens, half, k):
                return by_tiles(dst[:, half * P:(half + 1) * P], weights[:, k], half,
                                tokens[:, k].rearrange("p b t -> p (b t)"), start=(k == 0), stop=(k == HALVES - 1))

            def whole_array_piece(dst, weights, tokens, half, k):
                return nc.tensor.matmul(dst[:, half * P:(half + 1) * P], weights[:, k, half * P:(half + 1) * P],
                                        tokens[:, k].rearrange("p b t -> p (b t)"),
                                        start=(k == 0), stop=(k == HALVES - 1))

            pe.wait_ge(zeros_set, 1)
            for half in range(HALVES):
                for parity in range(2):
                    for q in range(QUADS):
                        last = nc.tensor.matmul(z[half][parity][Q * q:Q * (q + 1), 0:PAD + SLOTS * B], zeros[:, 0:Q],
                                                zeros[:, 0:PAD + SLOTS * B], start=True, stop=True,
                                                tile_position=(0, Q * q))
            last.then_inc(z_opened, 1)

            stream_zeros(1280)
            pe.wait_ge(ident_ready, 1)
            pe.wait_ge(cond_loaded, DMA)
            for k in range(HALVES):
                last = nc.tensor.transpose(cond_ps[:, k * B:(k + 1) * B], cond_rows[:, k * P:(k + 1) * P],
                                           ident[0:B, 0:B])
            last.then_inc(cond_transposed, 1)
            stream_zeros(1408)
            pe.wait_ge(x_first_loaded, DMA)
            transpose_x(1)

            pe.wait_ge(ys_sq_ready, 1)
            pe.wait_ge(w0_sq_ready, 1)
            for half in range(HALVES):
                for k in range(HALVES):
                    last = by_tiles(energy_ps[:, half * B:(half + 1) * B], w0_sq[:, k], half, ys_sq[:, k],
                                    start=(k == 0), stop=(k == HALVES - 1))
            last.then_inc(energy_summed, 1)

            pe.wait_ge(xs_ready, 1)
            for half, k in PIECES:
                last = whole_array_piece(lin_ps, w0_sb, xs_t, half, k)
            last.then_inc(lin_summed, 1)
            stream_zeros(1536)
            pe.wait_ge(wx_loaded, DMA)
            for half, k in PIECES:
                if half == 0:
                    pe.wait_ge(x2_ready, k + 1)
                last = whole_array_piece(input_ps, wx_sb, x2_next, half, k)
            last.then_inc(input_summed, 1)
            pe.wait_ge(wh_loaded, DMA)
            pe.wait_ge(h_padded, 2)
            stream_zeros(1024)

            ORDERS = ([(0, 0), (0, 1), (1, 0), (1, 1)], [(0, 0), (1, 0), (0, 1), (1, 1)])

            def block(i, first, last_block):
                for s in range(L):
                    if first and s < 2:
                        pe.wait_ge(z_seeded, s + 1)
                    if s in (SEED_TAIL[0] + 1, SEED_TAIL[1] + 1):
                        pe.wait_ge(z_seeded, 4 * i + 3 + SEED_TAIL.index(s - 1))
                    if not last_block and s in (SEED_HEAD[0] + 1, SEED_HEAD[1] + 1):
                        pe.wait_ge(z_seeded, 4 * i + 5 + SEED_HEAD.index(s - 1))

                    h_end = PAD + B * ((s - 1) % L + 1)
                    z_end = PAD + B * (s // 2 + 1)
                    waited = set()
                    for k, half in ORDERS[s % 2]:
                        if k not in waited:
                            pe.wait_ge(h_ready[k], i * L + s + 1)
                            waited.add(k)
                        last = by_tiles(z[half][s % 2][:, z_end - WINDOW * B:z_end], wh_sb[:, k], half,
                                        h_t[:, k, h_end - WINDOW * B:h_end], start=False, stop=True,
                                        skip_group_check=True)
                        if k == HALVES - 1:
                            last.then_inc(z_ready[half], 1)

                    if last_block and s == L - 1:
                        continue
                    fill = FILL_EVEN if s % 2 == 0 else FILL_ODD
                    if not last_block:
                        if s == X_TRANSPOSE:
                            pe.wait_ge(x_loaded, DMA * (i + 1))
                            transpose_x(0)
                            fill = FILL_TRANSPOSES
                        if s == LINEAR[0]:
                            pe.wait_ge(xs_ready, i + 2)
                        if s == INPUT[0]:
                            pe.wait_ge(x2_ready, 2 * (i + 2))
                        if s in LINEAR:
                            last = piece_of_product(lin_ps, w0_sb, xs_t, *PIECES[LINEAR.index(s)])
                            fill = 0
                        if s in INPUT:
                            last = piece_of_product(input_ps, wx_sb, x2_next, *PIECES[INPUT.index(s)])
                            fill = 0
                        if s == LINEAR[-1]:
                            last.then_inc(lin_summed, 1)
                        if s == INPUT[-1]:
                            last.then_inc(input_summed, 1)
                    if not first and s == OUT_TRANSPOSE:
                        pe.wait_ge(sum_ready, 2 * i)
                        transpose_out()
                        fill = FILL_TRANSPOSES
                    stream_zeros(fill)

            blocks(pe, block)
            for half in range(HALVES):
                pe.wait_ge(sum_ready, 2 * BLOCKS + half)
                transpose_half(last_ps[half], half).then_inc(out_transposed, 1)

        @block_ctx.vector
        def _(dve):
            def cut(tile, lo, hi):
                return tile[:].rearrange("p h b t -> p (h b) t")[:, :, lo:hi]

            def per_column(tile):
                return tile[:].rearrange("p h (b o) -> p (h b) o", o=1).broadcast_to([P, HALVES * B, L])

            def scale_x(n):
                dve.wait_ge(x_t_ready, n)
                nc.vector.tensor_tensor(cut(xs_t, 0, L), cut(x_t, 0, L), per_column(ys), ALU.mult)\
                    .then_inc(xs_ready, 1)

            def make_x2(n):
                dve.wait_ge(lin_summed, n)
                for half in range(HALVES):
                    product = lin_ps[:, half * P:(half + 1) * P].rearrange("p (b t) -> p b t", t=L)
                    scale = demod[:, half].rearrange("p (b o) -> p b o", o=1).broadcast_to([P, B, L])
                    nc.vector.tensor_tensor(lin_t[:, half], product, scale, ALU.mult).then_inc(lin_ready, 1)
                for half in range(HALVES):
                    dve.wait_ge(lin_ready, 2 * n - 1 + half)
                    nc.vector.tensor_tensor(x2_next[:, half], lin_t[:, half], x_t[:, half], ALU.add)\
                        .then_inc(x2_ready, 1)

            def keep_x2(lo, hi):
                nc.vector.tensor_copy(cut(x2_now, lo, hi), cut(x2_next, lo, hi)).then_inc(x2_kept, 1)

            def add_half(half, lo, hi):
                h = h_t[:, half, PAD + B * lo:PAD + B * hi].rearrange("p (t b) -> p b t", b=B)
                return nc.vector.tensor_tensor(sum_t[:, half, :, lo:hi], x2_now[:, half, :, lo:hi], h, ALU.add)

            def add_out(lo, hi):
                for half in range(HALVES):
                    last = add_half(half, lo, hi)
                last.then_inc(sum_ready, 1)

            def seed(parity, lo, hi):
                for half in range(HALVES):
                    src = input_ps[:, half * P:(half + 1) * P].rearrange("p (b u v) -> p v u b", b=B, v=2)
                    dst = z[half][parity][:, PAD + B * lo // 2:PAD + B * hi // 2].rearrange("p (u b) -> p u b", b=B)
                    last = nc.vector.tensor_scalar(dst, src[:, parity, lo // 2:hi // 2], bias_t[:, half:half + 1],
                                                   None, ALU.add)
                last.then_inc(z_seeded, 1)

            def states_written(count):
                for ready in h_ready:
                    dve.wait_ge(ready, count)

            nc.vector.memset(zeros[:], 0.0).then_inc(zeros_set, 1)
            dve.wait_ge(cond_transposed, 1)
            nc.vector.tensor_scalar(ys[:].rearrange("p h b -> p (h b)"), cond_ps, float(D) ** -0.5,
                                    None, ALU.mult).then_inc(ys_ready, 1)
            dve.wait_ge(ys_ready, 1)
            nc.vector.tensor_tensor(ys_sq[:], ys[:], ys[:], ALU.mult).then_inc(ys_sq_ready, 1)
            for half in range(HALVES):
                nc.vector.tensor_copy(h_t[:, half, PAD + B * (L - 1):PAD + B * L],
                                      cond_ps[:, half * B:(half + 1) * B]).then_inc(h_ready[half], 1)
            dve.wait_ge(w0_loaded, DMA)
            nc.vector.tensor_tensor(w0_sq[:], w0_sb[:], w0_sb[:], ALU.mult).then_inc(w0_sq_ready, 1)
            scale_x(1)
            dve.wait_ge(energy_summed, 1)
            nc.vector.tensor_scalar(energy[:].rearrange("p h b -> p (h b)"), energy_ps, EPS, None,
                                    ALU.add).then_inc(energy_ready, 1)
            dve.wait_ge(demod_ready, 1)
            make_x2(1)
            dve.wait_ge(x2_ready, 2)
            keep_x2(0, HL)
            keep_x2(HL, L)
            dve.wait_ge(z_opened, 1)
            dve.wait_ge(input_summed, 1)
            dve.wait_ge(bias_loaded, DMA)
            for parity in range(2):
                seed(parity, 0, HL)

            def block(i, first, last_block):
                if not first:
                    states_written(i * L + 1)
                    dve.wait_ge(x2_kept, 2 * i + 1)
                    add_out(HL, L)
                for parity, s in enumerate(SEED_TAIL):
                    states_written(i * L + s + 1)
                    seed(parity, HL, L)
                if not first:
                    dve.wait_ge(sum_ready, 2 * i)
                    keep_x2(HL, L)
                if not last_block:
                    scale_x(i + 2)
                    dve.wait_ge(x2_kept, 2 * i + 2)
                    make_x2(i + 2)
                states_written(i * L + HL + 1)
                if not first:
                    dve.wait_ge(out_transposed, i)
                add_out(0, HL)
                if not last_block:
                    dve.wait_ge(x2_ready, 2 * (i + 2))
                    dve.wait_ge(sum_ready, 2 * i + 1)
                    keep_x2(0, HL)
                    dve.wait_ge(input_summed, i + 2)
                    for parity, s in enumerate(SEED_HEAD):
                        states_written(i * L + s + 1)
                        seed(parity, 0, HL)

            blocks(dve, block)
            dve.wait_ge(x2_kept, 2 * BLOCKS)
            for half in range(HALVES):
                dve.wait_ge(h_ready[half], T + 1)
                add_half(half, HL, L).then_inc(sum_ready, 1)
            dve.wait_ge(out_transposed, BLOCKS)
            nc.vector.tensor_copy(out_rows[:, 0:P], last_ps[0][:, 0:P]).then_inc(out_rows_ready, 1)

        @block_ctx.scalar
        def _(act):
            act.dma_start(w0_sb[:], split_rows(w0)).then_inc(w0_loaded, DMA)
            act.dma_start(wx_sb[:], split_rows(wx)).then_inc(wx_loaded, DMA)
            act.wait_ge(minus_half_set, 1)
            nc.scalar.activation(tanh_probe[:], minus_half[0:1, 0, 0:1], ACT.Tanh).then_inc(tanh_loaded, 1)

            def copy_x(n):
                act.wait_ge(x_transposed, n)
                nc.scalar.copy(x_t[:].rearrange("p h b t -> p (h b t)"), xt_ps).then_inc(x_t_ready, 1)

            def copy_out(n):
                act.wait_ge(out_transposed, n)
                nc.scalar.copy(out_rows[:], out_ps).then_inc(out_rows_ready, 1)

            copy_x(1)

            def block(i, first, last_block):
                for s in range(L):
                    h_at, z_at = PAD + B * s, PAD + B * (s // 2)
                    for half in range(HALVES):
                        act.wait_ge(z_ready[half], i * L + s + 1)
                        nc.scalar.activation(h_t[:, half, h_at:h_at + B], z[half][s % 2][:, z_at:z_at + B],
                                             ACT.Tanh).then_inc(h_ready[half], 1)
                    if not last_block and s == X_COPY:
                        copy_x(i + 2)
                    if not first and s == OUT_COPY:
                        copy_out(i)
                    if not first and s == OUT_FREE:
                        act.wait_ge(out_stored, DMA * i)

            blocks(act, block)
            act.wait_ge(out_transposed, BLOCKS + 1)
            nc.scalar.copy(out_rows[:, P:D], last_ps[1][:, P:D]).then_inc(out_rows_ready, 1)


_INS = ["x", "cond_1024", "L0_cond_weight", "L1_cond_Wx", "L1_cond_Wh", "L1_cond_b"]
_OUTS = [((4, 512, 256), "float32")]


def kernel(**inputs):
    import numpy as _np
    import concourse.bacc as _bacc
    from concourse import mybir as _mybir
    from concourse.bass_utils import run_bass_kernel_spmd as _run

    nc = _bacc.Bacc("TRN2", target_bir_lowering=False, num_devices=1)
    arrays, args = {}, []
    for name in _INS:
        a = _np.ascontiguousarray(inputs[name])
        arrays[f"in_{name}_dram"] = a
        args.append(nc.dram_tensor(f"in_{name}_dram", a.shape, _mybir.dt.from_np(a.dtype), kind="ExternalInput").ap())
    for i, (shape, dtype) in enumerate(_OUTS):
        dt = _mybir.dt.from_np(_np.dtype(dtype))
        args.append(nc.dram_tensor(f"out_{i}_dram", shape, dt, kind="ExternalOutput").ap())
    build_cond_residual_rnn(nc, *args)
    r = _run(nc, [arrays], core_ids=[0])
    return r.results[0]["out_0_dram"]
```
